# Optimizing a Trainium2 kernel written in Bass

```python
import numpy as np
import jax
import jax.numpy as jnp

def _softmax(x, axis=-1):
    return jax.nn.softmax(x, axis=axis)

def _gelu(x):
    return jax.nn.gelu(x, approximate=True)

def _silu(x):
    return jax.nn.silu(x)

def _sigmoid(x):
    return jax.nn.sigmoid(x)

def _layernorm(x, axis=-1, eps=1e-05):
    m = jnp.mean(x, axis=axis, keepdims=True)
    v = jnp.var(x, axis=axis, keepdims=True)
    return (x - m) / jnp.sqrt(v + eps)

def _scatter_add(tgt, idx, src, axis=0):
    return tgt.at[idx].add(src)

def _segment_sum(src, seg, n):
    return jax.ops.segment_sum(src, seg, n)
kernel_name = 'mk_adj_ffn_d1_adj_r2_b2f73f'

def setup_inputs(seed: int=0):
    np.random.seed(seed)
    _w = jnp.asarray

    def _rec_inputs():
        import jax
        import jax.numpy as jnp
        _gk = jax.random.key(seed)
        x = -0.0002928 + 1 * jax.random.normal(jax.random.fold_in(_gk, 1), (1354, 256), jnp.float32)
        _a = jax.random.bernoulli(jax.random.fold_in(_gk, 2), 0.0118168, (1354, 1354))
        _a = jnp.logical_or(_a, jnp.swapaxes(_a, -1, -2))
        _a = jnp.logical_or(_a, jnp.eye(1354, dtype=bool))
        _af = _a.astype(jnp.float32)
        adj = _af
        return (x, adj)
    x, adj = _rec_inputs()

    def _L0_gnn_setup():
        import jax, jax.numpy as jnp
        import numpy as np
        N = 4096
        F_IN = 256
        F_OUT = 256
        DENSITY = 0.01
        key = jax.random.key(seed)
        k_x, k_adj, k_w, k_b = jax.random.split(key, 4)
        input_features = jax.random.normal(k_x, (N, F_IN), dtype=jnp.float32)
        adj = (jax.random.uniform(k_adj, (N, N)) < DENSITY).astype(jnp.float32)
        idx = jnp.arange(N)
        adj = adj.at[idx, idx].set(1.0)
        W = jax.random.normal(k_w, (F_IN, F_OUT), dtype=jnp.float32) / np.sqrt(F_IN)
        b = jax.random.normal(k_b, (F_OUT,), dtype=jnp.float32) * 0.01
        return {'input_features': input_features, 'adj': adj, 'W': W, 'b': b}
    _L0_gnn_all = _L0_gnn_setup()
    _L0_gnn_in = {k: v for k, v in _L0_gnn_all.items() if k in ('W', 'b')}
    del _L0_gnn_all

    def _L0_ffn_setup():
        import jax, jax.numpy as jnp
        import numpy as np
        D_MODEL = 256
        D_FF = 1024
        N_EXPERTS = 8
        TOP_K = 2
        key = jax.random.key(seed)
        ks = jax.random.split(key, 6)
        x = jax.random.normal(ks[0], (4, 512, D_MODEL), dtype=jnp.float32)
        router_w = jax.random.normal(ks[1], (N_EXPERTS, D_MODEL), dtype=jnp.float32) * 0.02
        lim1 = float(np.sqrt(6.0 / (D_FF + D_MODEL)))
        w1 = jax.random.uniform(ks[2], (N_EXPERTS, D_FF, D_MODEL), minval=-lim1, maxval=lim1, dtype=jnp.float32)
        b1 = jnp.zeros((N_EXPERTS, D_FF), dtype=jnp.float32)
        lim2 = float(np.sqrt(6.0 / (D_MODEL + D_FF)))
        w2 = jax.random.uniform(ks[3], (N_EXPERTS, D_MODEL, D_FF), minval=-lim2, maxval=lim2, dtype=jnp.float32)
        b2 = jnp.zeros((N_EXPERTS, D_MODEL), dtype=jnp.float32)
        return {'x': x, 'router_w': router_w, 'w1': w1, 'b1': b1, 'w2': w2, 'b2': b2}
    _L0_ffn_all = _L0_ffn_setup()
    _L0_ffn_in = {k: v for k, v in _L0_ffn_all.items() if k in ('router_w', 'w1', 'b1', 'w2', 'b2')}
    del _L0_ffn_all
    return {'x': x, 'adj': adj, 'L0_gnn_W': _L0_gnn_in['W'], 'L0_gnn_b': _L0_gnn_in['b'], 'L0_ffn_router_w': _L0_ffn_in['router_w'], 'L0_ffn_w1': _L0_ffn_in['w1'], 'L0_ffn_b1': _L0_ffn_in['b1'], 'L0_ffn_w2': _L0_ffn_in['w2'], 'L0_ffn_b2': _L0_ffn_in['b2']}

def reference(x, adj, L0_gnn_W, L0_gnn_b, L0_ffn_router_w, L0_ffn_w1, L0_ffn_b1, L0_ffn_w2, L0_ffn_b2):
    import jax
    import jax.numpy as jnp

    def _L0_gnn_ref(input_features, adj, W, b):
        import jax, jax.numpy as jnp
        import numpy as np
        N = 4096
        F_IN = 256
        F_OUT = 256
        DENSITY = 0.01
        A = (adj != 0).astype(input_features.dtype)
        hidden = input_features @ W + b
        deg = jnp.sum(A, axis=0)
        return A @ hidden / deg[:, None]

    def _L0_ffn_ref(x, router_w, w1, b1, w2, b2):
        import jax, jax.numpy as jnp
        import numpy as np
        D_MODEL = 256
        D_FF = 1024
        N_EXPERTS = 8
        TOP_K = 2
        router_logits = jnp.einsum('bnc,ec->bne', x, router_w)
        router_probs = jax.nn.softmax(router_logits, axis=-1)
        expert_weights, expert_indices = jax.lax.top_k(router_probs, TOP_K)
        expert_weights = expert_weights / (jnp.sum(expert_weights, axis=-1, keepdims=True) + 1e-09)
        hidden = jnp.einsum('bnc,edc->bned', x, w1) + b1
        hidden = jax.nn.gelu(hidden, approximate=False)
        expert_outputs = jnp.einsum('bned,ecd->bnec', hidden, w2) + b2
        idx = expert_indices[..., None]
        selected = jnp.take_along_axis(expert_outputs, idx, axis=2)
        output = jnp.sum(selected * expert_weights[..., None], axis=2)
        return output
    x = x + _L0_gnn_ref(_layernorm(x, axis=-1), adj, L0_gnn_W, L0_gnn_b)
    x = x + _L0_ffn_ref(_layernorm(x, axis=-1)[None], L0_ffn_router_w, L0_ffn_w1, L0_ffn_b1, L0_ffn_w2, L0_ffn_b2)[0]
    return x

_drawn_inputs = setup_inputs


def setup_inputs(seed=0):
    import zlib

    import numpy as np

    out = dict(_drawn_inputs(seed))
    spreads = {'L0_ffn_b1': (0.0, 0.1), 'L0_ffn_b2': (0.0, 0.1)}
    factors = {}
    for name, (base, spread) in spreads.items():
        noise = np.random.default_rng([zlib.crc32(name.encode()), seed]).standard_normal(out[name].shape)
        drawn = base * np.exp(spread * noise) if base else spread * noise
        out[name] = jnp.asarray(drawn.astype(out[name].dtype))
    for name, factor in factors.items():
        out[name] = (out[name] * factor).astype(out[name].dtype)
    return out
```

```python
import concourse.bass as bass
from concourse import mybir
from contextlib import ExitStack


def moe_gnn_kernel(nc: bass.Bass, x, adj_t, gnn_w, gnn_b, router_t, experts, b1_t, b2, out):
    fp32, fp16, bf16, i32, u32 = mybir.dt.float32, mybir.dt.float16, mybir.dt.bfloat16, mybir.dt.int32, mybir.dt.uint32
    ALU = mybir.AluOpType
    ACT = mybir.ActivationFunctionType
    AX = mybir.AxisListType

    P = 128
    N, D = x.shape
    E, _, FD = experts.shape
    CH = D // P
    FF = FD // (2 * CH)
    FJ = FF // P
    NB = -(-N // P)
    LAST = N - (NB - 1) * P
    NP = NB * P
    TOPK = 2
    NT = (TOPK * N + E * (P - 1)) // P
    CW = 1024
    CPE = FD // CW
    NCH = E * CPE
    RING = 4
    ARING = 3
    EPS = 1e-5
    WS = 256.0
    DUMMY = TOPK * NP
    COLS = [(s, min(512, N - s)) for s in range(0, N, 512)]
    GROUPS = [list(range(g, min(g + 4, NB))) for g in range(0, NB, 4)]

    def rows(b):
        return LAST if b == NB - 1 else P

    xn_dram = nc.dram_tensor("xn_rows", [NP, 2 * D], fp16, kind="Internal").ap()
    y_dram = nc.dram_tensor("y_rows", [DUMMY + P, D], fp32, kind="Internal").ap()

    ctx = ExitStack()
    with ctx:
        def sb(name, shape, dt):
            return ctx.enter_context(nc.sbuf_tensor(name, shape, dt))

        def sem(name):
            return ctx.enter_context(nc.semaphore(name))

        w1 = [sb("w1_high", [P, E, CH, FF], fp16), sb("w1_low", [P, E, CH, FF], bf16)]
        w2 = [sb("w2_high", [P, E, FJ, D], fp16), sb("w2_low", [P, E, FJ, D], bf16)]
        stage = sb("stage", [P, RING, CW], fp32)
        x_sb = sb("x_sb", [P, NB, D], fp32)
        arena_a = sb("arena_a", [P, 4096], fp32)
        adj_in = arena_a[:, 0:ARING * N].rearrange("p (r n) -> p r n", r=ARING)
        ax_t = arena_a[:, 0:CH * N].rearrange("p (c n) -> p c n", c=CH)
        hid = arena_a[:, 0:2 * FF].rearrange("p (s f) -> p s f", s=2)
        hid_pair = arena_a[:, 2 * FF:4 * FF].bitcast(fp16).rearrange("p (s h f) -> p s h f", s=2, h=2)
        arena_b = sb("arena_b", [P, 4096], fp16)
        adj01 = arena_b[:, 0:ARING * N].rearrange("p (r n) -> p r n", r=ARING)
        Q = TOPK * NB
        hot_row = arena_b[:, 0:Q * P].rearrange("p (q s) -> p q s", q=Q)
        hot_tile = arena_b[:, Q * P:Q * P + Q * 2 * NT].rearrange("p (q v t) -> p q v t", q=Q, v=2)
        xg = arena_b[:, 0:4 * D].rearrange("p (s d) -> p s d", s=2)
        xg_t = arena_b[:, 4 * D:8 * D].rearrange("p (s h t) -> p s h t", s=2, h=2 * CH)
        y_out = arena_b[:, 8 * D:12 * D].bitcast(fp32).rearrange("p (s d) -> p s d", s=2)
        xn = sb("xn", [P, NB, 2, D], fp16)
        xnf = sb("xnf", [P, 2, D], fp32)
        xn_t = sb("xn_t", [P, 2, CH, P], fp32)
        b2_all = xn[:, :, :, :].rearrange("p b h d -> p (b h d)")[:, 0:2 * E * D].bitcast(fp32) \
            .rearrange("p (e d) -> p e d", e=E)
        bias_row = sb("bias_row", [P, D], fp32)
        w_sb = sb("w_sb", [P, CH, D], fp32)
        rw_sb = sb("rw_sb", [P, CH, E], fp32)
        b1_sb = sb("b1_sb", [P, E, FJ], fp32)
        tmp_b = sb("tmp_b", [P, D], fp32)
        y_back = w1[0][:, :, :, :].rearrange("p e c f -> p (e c f)")[:, 0:NB * TOPK * D * 2] \
            .bitcast(fp32).rearrange("p (b k d) -> p b k d", b=NB, k=TOPK)

        ident = sb("ident", [P, P], fp32)
        ident16 = sb("ident16", [P, P], fp16)
        upper = sb("upper", [P, P], fp16)
        ones16 = sb("ones16", [P, P], fp16)
        iota_i = sb("iota_i", [P, P], i32)
        iota_f = sb("iota_f", [P, P], fp32)
        tok_i = sb("tok_i", [P, NB], i32)
        tok1 = sb("tok1", [P, NB], fp32)
        valid = sb("valid", [P, NB], fp32)
        row_i = sb("row_i", [P, 1], i32)
        row_f = sb("row_f", [P, 1], fp32)

        stats = sb("stats", [P, NB, 6], fp32)
        mv = sb("mv", [P, NB, 2], fp32)
        ve = sb("ve", [P, NB], fp32)
        sd = sb("sd", [P, NB], fp32)
        rstd = sb("rstd", [P, NB], fp32)
        nwt = sb("nwt", [P, 2, NB], fp32)
        deg = sb("deg", [P, NB], fp32)
        rdeg = sb("rdeg", [P, NB], fp32)
        rsum_d = sb("rsum_d", [P, NB], fp32)
        lg = sb("lg", [P, NB, E], fp32)
        mx = sb("mx", [P, NB, 8], fp32)
        ix = sb("ix", [P, NB, 8], u32)
        ixf = sb("ixf", [P, TOPK, NB], fp32)
        hot_e = sb("hot_e", [P, TOPK, NB, E], fp32)
        both = sb("both", [P, NB, E], fp16)
        eterm = sb("eterm", [P, NB, E + TOPK], fp32)
        zsum = sb("zsum", [P, NB], fp32)
        den = sb("den", [P, NB], fp32)
        gate = sb("gate", [P, NB, TOPK], fp32)
        cnt_i = sb("cnt_i", [P, 2, E], i32)
        ntile = sb("ntile", [P, E], fp32)
        ones_e = sb("ones_e", [P, E], fp32)
        tend = sb("tend", [P, E], fp32)
        base = sb("base", [P, E], fp32)
        pos = sb("pos", [P, NB, E], fp32)
        pos_k = arena_a[:, 3072:3072 + Q * E].rearrange("p (k b e) -> p k b e", k=TOPK, b=NB)
        slot = sb("slot", [P, Q], fp32)
        slot_i = sb("slot_i", [P, 3, Q], i32)
        slot_f = sb("slot_f", [P, 2, Q], fp32)
        ids = sb("ids", [P, 2, NT], fp32)
        empty = sb("empty", [P, NT], fp32)
        src_f = sb("src_f", [P, 2, NT], fp32)
        src_row = sb("src_row", [P, NT], i32)
        dst_row = sb("dst_row", [P, NT], i32)
        cmp_e = arena_a[0:1, CH * N:CH * N + NT * E].rearrange("p (t e) -> p t e", t=NT)
        exp_f = sb("exp_f", [1, NT], fp32)
        tile_exp = sb("tile_exp", [1, NT], i32)

        bank = [ctx.enter_context(nc.psum_tensor(f"bank{i}", [P, 512], fp32)) for i in range(8)]
        rs_ps = bank[6]
        g_ps = [bank[0], bank[7]]
        lg_ps = [bank[i][:, 0:NB * E].rearrange("p (b e) -> p b e", b=NB) for i in (4, 5, 1)]
        rank_ps = bank[5][:, 0:NB * E].rearrange("p (b e) -> p b e", b=NB)
        tot_ps = bank[7][:, 0:E]
        ids_ps = bank[6][:, 0:2 * NT].rearrange("p (v t) -> p v t", v=2)
        tr_ps = [bank[4 + s][:, :].bitcast(fp16)[:, 0:4 * P].rearrange("p (h t) -> p h t", h=4) for s in range(2)]
        y_ps = [bank[6 + s][:, 0:D] for s in range(2)]

        def hid_ps(s, j):
            return bank[2 * s + j // 4][:, (j % 4) * P:(j % 4 + 1) * P]

        x_in = sem("x_in")
        small_in = sem("small_in")
        adj_arrived = [sem(f"adj_arrived{r}") for r in range(ARING)]
        w_arrived = [sem(f"w_arrived{r}") for r in range(RING)]
        pad_zeroed = sem("pad_zeroed")
        const_step = sem("const_step")
        const_ready = sem("const_ready")
        dve_step = sem("dve_step")
        var_ready = sem("var_ready")
        sd_ready = sem("sd_ready")
        xnf_ready = sem("xnf_ready")
        xn_hi = sem("xn_hi")
        xn_lo = sem("xn_lo")
        adj_ready = sem("adj_ready")
        adj_used = sem("adj_used")
        ax_done = sem("ax_done")
        ax_act = sem("ax_act")
        ax_dve = sem("ax_dve")
        rs_done = sem("rs_done")
        rsum_ready = sem("rsum_ready")
        pool_step = sem("pool_step")
        xb_ready = sem("xb_ready")
        g_done = sem("g_done")
        g_used = sem("g_used")
        xt_done = sem("xt_done")
        xt_ready = sem("xt_ready")
        lg_done = sem("lg_done")
        exp_in = sem("exp_in")
        exp_done = sem("exp_done")
        both_ready = sem("both_ready")
        rank_done = sem("rank_done")
        hot_ready = sem("hot_ready")
        ids_done = sem("ids_done")
        route_ready = sem("route_ready")
        xn_stored = sem("xn_stored")
        b2_in = sem("b2_in")
        w_hi = sem("w_hi")
        w_lo = sem("w_lo")
        gathered = [sem(f"gathered{s}") for s in range(2)]
        tr_done = sem("tr_done")
        xg_ready = sem("xg_ready")
        hid_done = sem("hid_done")
        gelu_done = sem("gelu_done")
        hid_hi = sem("hid_hi")
        hid_ready = sem("hid_ready")
        y_done = sem("y_done")
        y_ready = sem("y_ready")
        scattered = [sem(f"scattered{s}") for s in range(2)]
        y_back_in = [sem(f"y_back_in{b}") for b in range(NB)]
        out_ready = sem("out_ready")
        stored = sem("stored")

        def w_chunk(n, part):
            e, q = n // CPE, n % CPE
            half = w1 if q < CPE // 2 else w2
            return half[part][:, e].rearrange("p a b -> p (a b)")[:, (q % (CPE // 2)) * CW:(q % (CPE // 2) + 1) * CW]

        def for_tiles(eng, step):
            for t in range(3):
                step(t, t % 2)
            pairs = (NT - 1 - 3) // 2
            with eng.Fori(0, pairs) as i:
                step(i * 2 + 3, 1)
                step(i * 2 + 4, 0)
            for t in range(3 + 2 * pairs, NT):
                step(t, t % 2)

        def known(t, n):
            return not isinstance(t, int) or t >= n

        def is_last(t, n=1):
            return isinstance(t, int) and t + n >= NT

        block = ctx.enter_context(nc.Block())

        @block.sync
        def _(sp):
            sp.dma_start(x_sb[:, 0:NB - 1, :],
                         x[0:(NB - 1) * P, :].rearrange("(b p) d -> p b d", p=P)).then_inc(x_in, 16)
            sp.wait_ge(pad_zeroed, 1)
            sp.dma_start(x_sb[0:LAST, NB - 1, :], x[(NB - 1) * P:N, :]).then_inc(x_in, 16)
            for b in range(NB):
                if b >= ARING:
                    sp.wait_ge(adj_ready, b - ARING + 1)
                sp.dma_start(adj_in[0:rows(b), b % ARING, :],
                             adj_t[b * P:b * P + rows(b), :]).then_inc(adj_arrived[b % ARING], 16)
            for n in range(NCH):
                if n >= RING:
                    sp.wait_ge(w_lo, n - RING + 1)
                sp.dma_start(stage[:, n % RING, :],
                             experts[n // CPE, :, (n % CPE) * CW:(n % CPE + 1) * CW]
                             ).then_inc(w_arrived[n % RING], 16)
            for s in range(2):
                sp.wait_ge(scattered[s], 16 * len(range(s, NT, 2)))
            for b in range(NB):
                for k in range(TOPK):
                    sp.dma_start(y_back[0:rows(b), b, k, :],
                                 y_dram[k * NP + b * P:k * NP + b * P + rows(b), :]).then_inc(y_back_in[b], 16)

        @block.gpsimd
        def _(pool):
            pool.memset(x_sb[:, NB - 1, :], 0.0).then_inc(pad_zeroed, 1)
            pool.memset(ident[:, :], 0.0).then_inc(const_step, 1)
            pool.memset(ident16[:, :], 0.0).then_inc(const_step, 1)
            pool.memset(upper[:, :], 0.0).then_inc(const_step, 1)
            pool.memset(ones16[:, :], 1.0).then_inc(const_step, 1)
            pool.memset(ones_e[:, :], 1.0).then_inc(const_step, 1)
            pool.iota(iota_i[:, :], pattern=[[1, P]], base=0, channel_multiplier=0).then_inc(const_step, 1)
            pool.iota(tok_i[:, :], pattern=[[P, NB]], base=1, channel_multiplier=1).then_inc(const_step, 1)
            pool.iota(row_i[:, :], pattern=[[1, 1]], base=DUMMY + 1, channel_multiplier=1).then_inc(const_step, 1)
            pool.wait_ge(const_step, 8)
            pool.affine_select(out=ident[:, :], in_=ident[:, :], compare_op=ALU.not_equal, fill=1.0,
                               base=0, pattern=[[-1, P]], channel_multiplier=1).then_inc(const_step, 1)
            pool.affine_select(out=ident16[:, :], in_=ident16[:, :], compare_op=ALU.not_equal, fill=1.0,
                               base=0, pattern=[[-1, P]], channel_multiplier=1).then_inc(const_step, 1)
            pool.affine_select(out=upper[:, :], in_=upper[:, :], compare_op=ALU.is_ge, fill=1.0,
                               base=0, pattern=[[-1, P]], channel_multiplier=1).then_inc(const_step, 1)
            pool.tensor_copy(iota_f[:, :], iota_i[:, :]).then_inc(const_step, 1)
            pool.tensor_copy(tok1[:, :], tok_i[:, :]).then_inc(const_step, 1)
            pool.tensor_copy(row_f[:, :], row_i[:, :]).then_inc(const_step, 1)
            pool.wait_ge(const_step, 14)
            pool.tensor_scalar(valid[:, :], tok1[:, :], float(N), None, ALU.is_le).then_inc(const_ready, 1)

            def split_low(n):
                pool.wait_ge(w_hi, n + 1)
                pool.tensor_tensor(w_chunk(n, 1), stage[:, n % RING, :], w_chunk(n, 0),
                                   ALU.subtract).then_inc(w_lo, 1)

            for n in range(8):
                split_low(n)
            pool.wait_ge(rsum_ready, 1)
            pool.wait_ge(small_in, 16 * 4)
            for b in range(NB):
                if b:
                    pool.wait_ge(xb_ready, b)
                pool.tensor_scalar(tmp_b[:, :], bias_row[:, :], rsum_d[:, b:b + 1], None,
                                   ALU.mult).then_inc(pool_step, 1)
                pool.wait_ge(pool_step, b + 1)
                pool.tensor_tensor(x_sb[:, b, :], x_sb[:, b, :], tmp_b[:, :], ALU.add).then_inc(xb_ready, 1)
            for n in range(8, NCH):
                split_low(n)

            pool.wait_ge(route_ready, 1)
            pool.wait_ge(xn_stored, 16 * NB)

            def gather(t):
                pool.indirect_dma_start(xg[:, t % 2, :], None, xn_dram[:, :],
                                        bass.IndirectOffsetOnAxis(src_row[:, t:t + 1], 0)
                                        ).then_inc(gathered[t % 2], 16)

            gather(0)
            gather(1)
            for t in range(NT):
                if t + 2 < NT:
                    pool.wait_ge(tr_done, t + 1)
                    gather(t + 2)
                pool.wait_ge(y_ready, t + 1)
                if t >= 1:
                    pool.wait_ge(scattered[(t - 1) % 2], 16 * ((t - 1) // 2 + 1))
                pool.indirect_dma_start(y_dram[:, :], bass.IndirectOffsetOnAxis(dst_row[:, t:t + 1], 0),
                                        y_out[:, t % 2, :], None).then_inc(scattered[t % 2], 16)

        @block.scalar
        def _(act):
            for dst, src in ((w_sb[:, :, :], gnn_w.rearrange("(c p) d -> p c d", p=P)),
                             (rw_sb[:, :, :], router_t.rearrange("(c p) e -> p c e", p=P)),
                             (b1_sb[:, :, :], b1_t),
                             (bias_row[:, :], gnn_b.partition_broadcast(P))):
                act.dma_start(dst, src).then_inc(small_in, 16)
            act.wait_ge(var_ready, 1)
            act.activation(sd[:, :], ve[:, :], ACT.Sqrt).then_inc(sd_ready, 1)
            for b in range(NB):
                act.wait_ge(xnf_ready, b + 1)
                act.activation(xn[:, b, 0, :], xnf[:, b % 2, :], ACT.Copy).then_inc(xn_hi, 1)

            def split_high(n):
                act.wait_ge(w_arrived[n % RING], 16 * (n // RING + 1))
                act.activation(w_chunk(n, 0), stage[:, n % RING, :], ACT.Copy).then_inc(w_hi, 1)

            for n in range(8):
                split_high(n)
            for i, (c, w) in enumerate(COLS):
                act.wait_ge(ax_done, 2 * i + 1)
                act.activation(ax_t[:, 0, c:c + w], bank[i][:, 0:w], ACT.Copy).then_inc(ax_act, 1)

            def root(g):
                act.wait_ge(var_ready, g + 2)
                blocks = GROUPS[g]
                act.activation(sd[:, blocks[0]:blocks[-1] + 1], ve[:, blocks[0]:blocks[-1] + 1],
                               ACT.Sqrt).then_inc(sd_ready, 1)

            def normed(b):
                act.wait_ge(xnf_ready, NB + b + 1)
                if b == 0:
                    act.wait_ge(ax_done, 2 * len(COLS))
                act.activation(xn[:, b, 0, :], xnf[:, b % 2, :], ACT.Copy).then_inc(xn_hi, 1)
                act.wait_ge(xt_done, b + 1)
                if b >= 2:
                    act.wait_ge(lg_done, b - 1)
                act.activation(xn_t[:, b % 2, :, :].rearrange("p c t -> p (c t)"), bank[2 + b % 2][:, 0:D],
                               ACT.Copy).then_inc(xt_ready, 1)
                act.wait_ge(xn_lo, NB + b + 1)
                act.dma_start(xn_dram[b * P:(b + 1) * P, :],
                              xn[:, b, :, :].rearrange("p h d -> p (h d)")).then_inc(xn_stored, 16)

            root(0)
            root(1)
            for g, blocks in enumerate(GROUPS):
                if g + 1 >= 2 and g + 1 < len(GROUPS):
                    root(g + 1)
                for b in blocks:
                    normed(b)
            act.wait_ge(xn_stored, 16 * NB)
            act.dma_start(b2_all, b2.partition_broadcast(P)).then_inc(b2_in, 16)
            act.wait_ge(exp_in, 1)
            act.activation(eterm[:, :, :], eterm[:, :, :], ACT.Exp).then_inc(exp_done, 1)
            for n in range(8, NCH):
                split_high(n)
            act.wait_ge(route_ready, 1)

            def step(t, s):
                e = act.value_load(tile_exp[0:1, bass.ds(t, 1)], min_val=0, max_val=E - 1)
                if known(t, 2):
                    act.wait_ge(hid_ready, t - 1)
                for j in range(FJ):
                    if j % 4 == 0:
                        act.wait_ge(hid_done, t * 2 + (j // 4 + 1))
                    ins = act.activation(hid[:, s, j * P:(j + 1) * P], hid_ps(s, j), ACT.Gelu,
                                         bias=b1_sb[:, bass.ds(e, 1), j])
                ins.then_inc(gelu_done, 1)

            for_tiles(act, step)
            for b in range(NB):
                act.wait_ge(out_ready, b + 1)
                act.dma_start(out[b * P:b * P + rows(b), :], x_sb[0:rows(b), b, :]).then_inc(stored, 16)
            act.wait_ge(stored, 16 * NB)

        @block.vector
        def _(dve):
            steps = [0]

            def then(ins):
                steps[0] += 1
                ins.then_inc(dve_step, 1)
                dve.wait_ge(dve_step, steps[0])

            def newton(lo, hi):
                r, v = rstd[:, lo:hi], ve[:, lo:hi]
                a, c = nwt[:, 0, lo:hi], nwt[:, 1, lo:hi]
                then(dve.reciprocal(r, sd[:, lo:hi]))
                then(dve.tensor_tensor(a, r, r, ALU.mult))
                then(dve.tensor_tensor(c, a, v, ALU.mult))
                then(dve.tensor_scalar(a, c, -0.5, 1.5, ALU.mult, ALU.add))
                then(dve.tensor_tensor(r, r, a, ALU.mult))

            def normalize(b, n):
                if n >= 2:
                    dve.wait_ge(xn_hi, n - 1)
                    dve.wait_ge(xn_lo, n - 1)
                if n >= NB + 2:
                    dve.wait_ge(xt_done, n - NB - 1)
                dve.tensor_scalar(xnf[:, n % 2 if n < NB else b % 2, :], x_sb[:, b, :], mv[:, b, 0:1], rstd[:, b:b + 1],
                                  ALU.subtract, ALU.mult).then_inc(xnf_ready, 1)

            def low_part(b, n):
                dve.wait_ge(xn_hi, n + 1)
                dve.tensor_tensor(xn[:, b, 1, :], xnf[:, n % 2 if n < NB else b % 2, :], xn[:, b, 0, :],
                                  ALU.subtract).then_inc(xn_lo, 1)

            dve.memset(deg[:, :], 1.0).then_inc(dve_step, 1)
            steps[0] += 1
            dve.wait_ge(x_in, 32)
            for b in range(NB):
                ins = dve.bn_stats(stats[:, b, :], x_sb[:, b, :])
            then(ins)
            for b in range(NB):
                ins = dve.bn_aggr(mv[:, b, :], stats[:, b, :])
            then(ins)
            dve.tensor_scalar(ve[:, :], mv[:, :, 1], EPS, None, ALU.add).then_inc(var_ready, 1)
            dve.wait_ge(sd_ready, 1)
            newton(0, NB)
            normalize(0, 0)
            for b in range(NB):
                r = rows(b)
                if b + 1 < NB:
                    normalize(b + 1, b + 1)
                dve.wait_ge(adj_arrived[b % ARING], 16 * (b // ARING + 1))
                if b >= ARING:
                    dve.wait_ge(adj_used, b - ARING + 1)
                dve.tensor_scalar(adj01[0:r, b % ARING, :], adj_in[0:r, b % ARING, :], 0.0, 0.0,
                                  ALU.not_equal, ALU.add, accum_out=deg[0:r, b:b + 1]).then_inc(adj_ready, 1)
                low_part(b, b)
            dve.wait_ge(adj_ready, NB)
            then(dve.reciprocal(rdeg[:, :], deg[:, :]))
            for i, (c, w) in enumerate(COLS):
                dve.wait_ge(ax_done, 2 * i + 2)
                dve.tensor_copy(ax_t[:, 1, c:c + w], bank[3 + i][:, 0:w]).then_inc(ax_dve, 1)
                if i == 0:
                    dve.wait_ge(rs_done, 1)
                    then(dve.memset(rsum_d[:, :], 0.0))
                    dve.tensor_tensor(rsum_d[:, 0:NB - 1], rs_ps[:, 0:NB - 1], rdeg[:, 0:NB - 1], ALU.mult)
                    dve.tensor_tensor(rsum_d[0:LAST, NB - 1:NB], rs_ps[0:LAST, NB - 1:NB],
                                      rdeg[0:LAST, NB - 1:NB], ALU.mult).then_inc(rsum_ready, 1)

            def stage_a(g):
                for b in GROUPS[g]:
                    r = rows(b)
                    dve.wait_ge(xb_ready, b + 1)
                    dve.wait_ge(g_done, b + 1)
                    dve.scalar_tensor_tensor(x_sb[0:r, b, :], g_ps[b % 2][0:r, 0:D], rdeg[0:r, b:b + 1],
                                             x_sb[0:r, b, :], ALU.mult, ALU.add).then_inc(g_used, 1)
                    dve.wait_ge(g_used, b + 1)
                    ins = dve.bn_stats(stats[:, b, :], x_sb[:, b, :])
                then(ins)
                for b in GROUPS[g]:
                    ins = dve.bn_aggr(mv[:, b, :], stats[:, b, :])
                then(ins)
                lo, hi = GROUPS[g][0], GROUPS[g][-1] + 1
                dve.tensor_scalar(ve[:, lo:hi], mv[:, lo:hi, 1], EPS, None, ALU.add).then_inc(var_ready, 1)

            def stage_b(g):
                lo, hi = GROUPS[g][0], GROUPS[g][-1] + 1
                dve.wait_ge(sd_ready, g + 2)
                newton(lo, hi)
                normalize(lo, NB + lo)
                for b in GROUPS[g]:
                    if b + 1 < hi:
                        normalize(b + 1, NB + b + 1)
                    low_part(b, NB + b)

            def stage_c(g):
                lo, hi = GROUPS[g][0], GROUPS[g][-1] + 1
                dve.wait_ge(lg_done, hi)
                then(dve.tensor_copy(lg[:, lo:hi, :], lg_ps[g][:, lo:hi, :]))
                for b in GROUPS[g]:
                    then(dve.max(mx[:, b, :], lg[:, b, :]))
                    ins = dve.max_index(ix[:, b, :], mx[:, b, :], lg[:, b, :])
                then(ins)

            stage_a(0)
            stage_a(1)
            stage_b(0)
            stage_a(2)
            stage_b(1)
            stage_c(0)
            stage_b(2)
            stage_c(1)
            stage_c(2)

            dve.wait_ge(const_ready, 1)
            then(dve.tensor_copy(ixf[:, :, :], ix[:, :, 0:TOPK].rearrange("p b k -> p k b")))
            then(dve.tensor_tensor(hot_e[:, :, :, :],
                                   iota_f[:, 0:E].unsqueeze(1).unsqueeze(1).broadcast_to((P, TOPK, NB, E)),
                                   ixf[:, :, :].unsqueeze(3).broadcast_to((P, TOPK, NB, E)), ALU.is_equal))
            then(dve.tensor_tensor(pos[:, :, :], hot_e[:, 0], hot_e[:, 1], ALU.add))
            dve.tensor_tensor(both[:, :, :], pos[:, :, :], valid[:, :].unsqueeze(2).broadcast_to((P, NB, E)),
                              ALU.mult).then_inc(both_ready, 1)
            top = mx[:, :, 0:1]
            dve.tensor_tensor(eterm[:, :, 0:E], lg[:, :, :], top.broadcast_to((P, NB, E)), ALU.subtract)
            dve.tensor_tensor(eterm[:, :, E:E + TOPK], mx[:, :, 0:TOPK], top.broadcast_to((P, NB, TOPK)),
                              ALU.subtract).then_inc(exp_in, 1)
            dve.wait_ge(rank_done, 1)
            then(dve.tensor_scalar(cnt_i[:, 0, :], tot_ps, float(P - 1), None, ALU.add))
            then(dve.tensor_scalar(cnt_i[:, 1, :], cnt_i[:, 0, :], 7, None, ALU.arith_shift_right))
            then(dve.tensor_copy(ntile[:, :], cnt_i[:, 1, :]))
            then(dve.tensor_tensor_scan(tend[:, :], ones_e[:, :], ntile[:, :], 0.0, ALU.mult, ALU.add))
            then(dve.tensor_tensor(base[:, :], tend[:, :], ntile[:, :], ALU.subtract))
            then(dve.tensor_scalar(base[:, :], base[:, :], float(P), None, ALU.mult))
            then(dve.tensor_tensor(pos[:, :, :], rank_ps, base[:, :].unsqueeze(1).broadcast_to((P, NB, E)), ALU.add))
            then(dve.tensor_tensor(pos_k[:, :, :, :], hot_e[:, :, :, :],
                                   pos[:, :, :].unsqueeze(1).broadcast_to((P, TOPK, NB, E)), ALU.mult))
            then(dve.tensor_reduce(slot[:, :].rearrange("p (k b) -> p k b", k=TOPK), pos_k[:, :, :, :],
                                   AX.X, ALU.add))
            then(dve.tensor_copy(slot_i[:, 0, :], slot[:, :]))
            dve.tensor_scalar(slot_i[:, 1, :], slot_i[:, 0, :], 7, None, ALU.arith_shift_right)
            then(dve.tensor_scalar(slot_i[:, 2, :], slot_i[:, 0, :], P - 1, None, ALU.bitwise_and))
            then(dve.tensor_copy(slot_f[:, :, :], slot_i[:, 1:3, :]))
            dve.tensor_tensor(hot_row, iota_f[:, :].unsqueeze(1).broadcast_to((P, Q, P)),
                              slot_f[:, 1, :].unsqueeze(2).broadcast_to((P, Q, P)), ALU.is_equal)
            for v in range(2):
                ins = dve.tensor_tensor(hot_tile[:, :, v, :], iota_f[:, 0:NT].unsqueeze(1).broadcast_to((P, Q, NT)),
                                        slot_f[:, 0, :].unsqueeze(2).broadcast_to((P, Q, NT)), ALU.is_equal)
            then(ins)
            for k in range(TOPK):
                part = hot_tile[:, k * NB:(k + 1) * NB]
                dve.tensor_tensor(part[:, :, 0, :], part[:, :, 0, :],
                                  tok1[:, :].unsqueeze(2).broadcast_to((P, NB, NT)), ALU.mult)
                if k == 0:
                    dve.memset(part[:, :, 1, :], 0.0)
            then(dve.tensor_tensor(ids[:, 0, 0:NB], valid[:, :], valid[:, :], ALU.mult))
            for k in range(TOPK):
                part = hot_tile[:, k * NB + NB - 1]
                dve.tensor_scalar(part, part, valid[:, NB - 1:NB], None, ALU.mult).then_inc(hot_ready, 1)
            then(dve.tensor_tensor(cmp_e, iota_f[0:1, 0:NT].unsqueeze(2).broadcast_to((1, NT, E)),
                                   tend[0:1, :].unsqueeze(1).broadcast_to((1, NT, E)), ALU.is_ge))
            then(dve.tensor_reduce(exp_f[0:1, :], cmp_e, AX.X, ALU.add))
            then(dve.tensor_scalar(tile_exp[0:1, :], exp_f[0:1, :], float(E - 1), None, ALU.min))
            dve.wait_ge(ids_done, 1)
            then(dve.tensor_copy(ids[:, :, :], ids_ps))
            then(dve.tensor_scalar(src_f[:, 0, :], ids[:, 0, :], -1.0, 0.0, ALU.add, ALU.max))
            dve.tensor_copy(src_row[:, :], src_f[:, 0, :])
            then(dve.tensor_scalar(empty[:, :], ids[:, 0, :], 0.0, row_f[:, 0:1], ALU.is_equal, ALU.mult))
            then(dve.scalar_tensor_tensor(src_f[:, 1, :], ids[:, 1, :], float(NP), ids[:, 0, :], ALU.mult, ALU.add))
            then(dve.tensor_tensor(src_f[:, 1, :], src_f[:, 1, :], empty[:, :], ALU.add))
            dve.tensor_scalar(dst_row[:, :], src_f[:, 1, :], -1.0, None, ALU.add).then_inc(route_ready, 1)
            dve.wait_ge(exp_done, 1)
            then(dve.tensor_reduce(zsum[:, :], eterm[:, :, 0:E], AX.X, ALU.add))
            then(dve.tensor_tensor(den[:, :], eterm[:, :, E], eterm[:, :, E + 1], ALU.add))
            then(dve.scalar_tensor_tensor(den[:, :], zsum[:, :], 1e-9, den[:, :], ALU.mult, ALU.add))
            then(dve.reciprocal(den[:, :], den[:, :]))
            then(dve.tensor_tensor(gate[:, :, :], eterm[:, :, E:E + TOPK],
                                   den[:, :].unsqueeze(2).broadcast_to((P, NB, TOPK)), ALU.mult))

            def tokens_in(t, s):
                dve.wait_ge(tr_done, t + 1)
                if known(t, 2):
                    dve.wait_ge(hid_done, (t - 1) * 2)
                dve.tensor_copy(xg_t[:, s], tr_ps[s]).then_inc(xg_ready, 1)

            def results_out(t, s, e):
                dve.wait_ge(y_done, t + 1)
                if known(t, 2):
                    dve.wait_ge(scattered[s], scatters_before(t))
                dve.tensor_tensor(y_out[:, s, :], y_ps[s], b2_all[:, bass.ds(e, 1), :]
                                  .rearrange("p a d -> p (a d)"), ALU.add).then_inc(y_ready, 1)

            def scatters_before(t):
                return 16 * (t // 2) if isinstance(t, int) else t * 8 - (8 if odd[0] else 0)

            odd = [False]
            dve.wait_ge(b2_in, 16)
            tokens_in(0, 0)

            def step(t, s):
                if not is_last(t):
                    tokens_in(t + 1, 1 - s)
                dve.wait_ge(gelu_done, t + 1)
                if known(t, 2):
                    dve.wait_ge(y_done, t - 1)
                dve.tensor_copy(hid_pair[:, s, 0, :], hid[:, s, :]).then_inc(hid_hi, 1)
                dve.wait_ge(hid_hi, t + 1)
                dve.tensor_tensor(hid_pair[:, s, 1, :], hid[:, s, :], hid_pair[:, s, 0, :],
                                  ALU.subtract).then_inc(hid_ready, 1)
                if known(t, 1):
                    e = dve.value_load(tile_exp[0:1, bass.ds(t - 1, 1)], min_val=0, max_val=E - 1)
                    odd[0] = s == 0
                    results_out(t - 1, 1 - s, e)
                if is_last(t):
                    e = dve.value_load(tile_exp[0:1, t:t + 1], min_val=0, max_val=E - 1)
                    results_out(t, s, e)

            for_tiles(dve, step)
            for b in range(NB):
                r = rows(b)
                dve.wait_ge(y_back_in[b], 32)
                then(dve.scalar_tensor_tensor(x_sb[0:r, b, :], y_back[0:r, b, 0, :], gate[0:r, b, 0:1],
                                              x_sb[0:r, b, :], ALU.mult, ALU.add))
                dve.scalar_tensor_tensor(x_sb[0:r, b, :], y_back[0:r, b, 1, :], gate[0:r, b, 1:2],
                                         x_sb[0:r, b, :], ALU.mult, ALU.add).then_inc(out_ready, 1)

        @block.tensor
        def _(pe):
            pe.wait_ge(const_ready, 1)
            for b in range(NB):
                r = rows(b)
                pe.wait_ge(xn_lo, b + 1)
                pe.wait_ge(adj_ready, b + 1)
                for i, (c, w) in enumerate(COLS):
                    for ch in range(CH):
                        for part in range(2):
                            ins = pe.matmul(bank[3 * ch + i][:, 0:w], xn[0:r, b, part, ch * P:(ch + 1) * P],
                                            adj01[0:r, b % ARING, c:c + w],
                                            start=(b == 0 and part == 0), stop=(b == NB - 1 and part == 1))
                        if b == NB - 1:
                            ins.then_inc(ax_done, 1)
                for i in range(NB):
                    ins = pe.matmul(rs_ps[0:rows(i), i:i + 1], adj01[0:r, b % ARING, i * P:i * P + rows(i)],
                                    ones16[0:r, 0:1], start=(b == 0 and i == 0),
                                    stop=(b == NB - 1), skip_group_check=True)
                ins.then_inc(adj_used, 1)
            pe.wait_ge(adj_used, NB)
            pe.nop().then_inc(rs_done, 1)
            pe.wait_ge(small_in, 16 * 4)

            def graph(b):
                c = min(b // 4, len(COLS) - 1)
                pe.wait_ge(ax_act, c + 1)
                pe.wait_ge(ax_dve, c + 1)
                if b >= 2:
                    pe.wait_ge(g_used, b - 1)
                for ch in range(CH):
                    ins = pe.matmul(g_ps[b % 2][0:rows(b), 0:D], ax_t[:, ch, b * P:b * P + rows(b)], w_sb[:, ch, :],
                                    start=(ch == 0), stop=(ch == CH - 1))
                ins.then_inc(g_done, 1)

            def turn(b):
                if b == 0:
                    pe.wait_ge(ax_act, len(COLS))
                    pe.wait_ge(ax_dve, len(COLS))
                pe.wait_ge(xnf_ready, NB + b + 1)
                if b >= 2:
                    pe.wait_ge(xt_ready, b - 1)
                for ch in range(CH):
                    ins = pe.transpose(bank[2 + b % 2][:, ch * P:(ch + 1) * P], xnf[:, b % 2, ch * P:(ch + 1) * P],
                                       ident[:, :])
                ins.then_inc(xt_done, 1)

            def logits(b):
                pe.wait_ge(xt_ready, b + 1)
                for ch in range(CH):
                    ins = pe.matmul(lg_ps[b // 4][:, b, :], xn_t[:, b % 2, ch, :], rw_sb[:, ch, :],
                                    start=(ch == 0), stop=(ch == CH - 1))
                ins.then_inc(lg_done, 1)

            def route(g):
                for b in GROUPS[g]:
                    turn(b)
                    logits(b)

            for g in (0, 1):
                for b in GROUPS[g]:
                    graph(b)
            route(0)
            for b in GROUPS[2]:
                graph(b)
            route(1)
            route(2)
            pe.wait_ge(both_ready, 1)
            flat = both[:, :, :].rearrange("p b e -> p (b e)")
            flat_ps = bank[5][:, 0:NB * E]
            pe.matmul(flat_ps, upper[:, :], flat, start=True, stop=False, skip_group_check=True)
            for b in range(1, NB):
                pe.matmul(flat_ps[:, b * E:NB * E], ones16[:, :], flat[:, 0:(NB - b) * E],
                          start=False, stop=(b == NB - 1), skip_group_check=True)
            for b in range(NB):
                ins = pe.matmul(tot_ps, ones16[:, :], both[:, b, :], start=(b == 0), stop=(b == NB - 1))
            ins.then_inc(rank_done, 1)
            pe.wait_ge(hot_ready, 2)
            for q in range(Q):
                ins = pe.matmul(bank[6][:, 0:2 * NT], hot_row[:, q, :],
                                hot_tile[:, q].rearrange("p v t -> p (v t)"), start=(q == 0), stop=(q == Q - 1))
            ins.then_inc(ids_done, 1)
            pe.wait_ge(route_ready, 1)

            def turn_tokens(t, s, uses):
                pe.wait_ge(gathered[s], uses)
                if known(t, 2):
                    pe.wait_ge(xg_ready, t - 1)
                for h in range(2 * CH):
                    ins = pe.transpose(tr_ps[s][:, h, :], xg[:, s, h * P:(h + 1) * P], ident16[:, :])
                ins.then_inc(tr_done, 1)

            def layer1(t, s, e):
                pe.wait_ge(xg_ready, t + 1)
                pe.wait_ge(w_lo, e * CPE + CPE)
                if known(t, 2):
                    pe.wait_ge(gelu_done, t - 1)
                for j in range(FJ):
                    n = 0
                    for wp, xp in ((0, 0), (0, 1), (1, 0)):
                        for c in range(CH):
                            ins = pe.matmul(hid_ps(s, j), w1[wp][:, bass.ds(e, 1), c, j * P:(j + 1) * P]
                                            .rearrange("p a f -> p (a f)"),
                                            xg_t[:, s, xp * CH + c, :], start=(n == 0), stop=(n == 5))
                            n += 1
                    if j % 4 == 3:
                        ins.then_inc(hid_done, 1)

            def layer2(t, s, e):
                pe.wait_ge(hid_ready, t + 1)
                if known(t, 2):
                    pe.wait_ge(y_ready, t - 1)
                n = 0
                for j in range(FJ):
                    for hp, wp in ((0, 0), (0, 1), (1, 0)):
                        ins = pe.matmul(y_ps[s], hid_pair[:, s, hp, j * P:(j + 1) * P],
                                        w2[wp][:, bass.ds(e, 1), j, :].rearrange("p a d -> p (a d)"),
                                        start=(n == 0), stop=(n == 3 * FJ - 1))
                        n += 1
                ins.then_inc(y_done, 1)

            def step(t, s):
                e = pe.value_load(tile_exp[0:1, bass.ds(t, 1)], min_val=0, max_val=E - 1)
                layer1(t, s, e)
                if not is_last(t):
                    if isinstance(t, int):
                        uses = 16 * ((t + 1) // 2 + 1)
                    else:
                        uses = t * 8 + (24 if s == 1 else 16)
                    turn_tokens(t + 1, 1 - s, uses)
                if known(t, 1):
                    before = pe.value_load(tile_exp[0:1, bass.ds(t - 1, 1)], min_val=0, max_val=E - 1)
                    layer2(t - 1, 1 - s, before)
                if is_last(t):
                    layer2(t, s, e)

            turn_tokens(0, 0, 16)
            for_tiles(pe, step)


_OUT = ((1354, 256), "float32")


def kernel(x, adj, L0_gnn_W, L0_gnn_b, L0_ffn_router_w, L0_ffn_w1, L0_ffn_b1, L0_ffn_w2, L0_ffn_b2):
    import numpy as np
    import concourse.bacc as bacc
    from concourse.bass_utils import run_bass_kernel_spmd

    P = 128
    x, adj, w1, b1, w2 = (np.asarray(a) for a in (x, adj, L0_ffn_w1, L0_ffn_b1, L0_ffn_w2))
    E, FF, D = w1.shape
    w1_t = w1.transpose(0, 2, 1).reshape(E, D // P, P, FF).transpose(0, 2, 1, 3).reshape(E, P, -1)
    w2_t = w2.transpose(0, 2, 1).reshape(E, FF // P, P, D).transpose(0, 2, 1, 3).reshape(E, P, -1)
    arrays = {
        "in_x": np.ascontiguousarray(x),
        "in_adj_t": np.ascontiguousarray(adj.T),
        "in_gnn_w": np.ascontiguousarray(L0_gnn_W),
        "in_gnn_b": np.ascontiguousarray(L0_gnn_b),
        "in_router_t": np.ascontiguousarray(np.asarray(L0_ffn_router_w).T),
        "in_experts": np.ascontiguousarray(np.concatenate([w1_t, w2_t], axis=2)),
        "in_b1_t": np.ascontiguousarray(b1.reshape(E, FF // P, P).transpose(2, 0, 1)),
        "in_b2": np.ascontiguousarray(L0_ffn_b2),
    }
    nc = bacc.Bacc("TRN2", target_bir_lowering=False, num_devices=1)
    args = [nc.dram_tensor(n, a.shape, mybir.dt.from_np(a.dtype), kind="ExternalInput").ap()
            for n, a in arrays.items()]
    out = nc.dram_tensor("out", _OUT[0], mybir.dt.float32, kind="ExternalOutput").ap()
    moe_gnn_kernel(nc, *args, out)
    result = run_bass_kernel_spmd(nc, [arrays], core_ids=[0])
    return result.results[0]["out"]
```
